# Optimizing a Trainium2 kernel written in Bass

```python
import numpy as np
import jax
import jax.numpy as jnp

def _softmax(x, axis=-1):
    return jax.nn.softmax(x, axis=axis)

def _gelu(x):
    return jax.nn.gelu(x, approximate=True)

def _silu(x):
    return jax.nn.silu(x)

def _sigmoid(x):
    return jax.nn.sigmoid(x)

def _layernorm(x, axis=-1, eps=1e-05):
    m = jnp.mean(x, axis=axis, keepdims=True)
    v = jnp.var(x, axis=axis, keepdims=True)
    return (x - m) / jnp.sqrt(v + eps)

def _scatter_add(tgt, idx, src, axis=0):
    return tgt.at[idx].add(src)

def _segment_sum(src, seg, n):
    return jax.ops.segment_sum(src, seg, n)
kernel_name = 'mk_adj_preln_d4_adj_r2_e82a8a'

def setup_inputs(seed: int=0):
    np.random.seed(seed)
    _w = jnp.asarray

    def _rec_inputs():
        import jax
        import jax.numpy as jnp
        _gk = jax.random.key(seed)
        x = -5.207e-06 + 0.01001 * jax.random.normal(jax.random.fold_in(_gk, 1), (4096, 128), jnp.float32)
        _a = jax.random.bernoulli(jax.random.fold_in(_gk, 2), 0.00195312, (4096, 4096))
        _a = jnp.logical_or(_a, jnp.eye(4096, dtype=bool))
        _af = _a.astype(jnp.float32)
        _af = _af / jnp.maximum(_af.sum(-1, keepdims=True), 1.0)
        adj = _af
        return (x, adj)
    x, adj = _rec_inputs()

    def _L0_gnn_setup():
        import jax, jax.numpy as jnp
        import numpy as np
        MIN_NORM = 1e-15
        BALL_EPS = 0.004
        C_IN = 1.0
        C_OUT = 1.0

        def _norm(x):
            return jnp.clip(jnp.linalg.norm(x, axis=-1, keepdims=True), MIN_NORM, None)

        def artanh(x):
            return jnp.arctanh(jnp.clip(x, -1.0 + 1e-07, 1.0 - 1e-07))

        def proj(x, c):
            norm = _norm(x)
            maxnorm = (1.0 - BALL_EPS) / jnp.sqrt(c)
            return jnp.where(norm > maxnorm, x / norm * maxnorm, x)

        def expmap0(u, c):
            sc = jnp.sqrt(c)
            un = _norm(u)
            return jnp.tanh(sc * un) * u / (sc * un)

        def logmap0(p, c):
            sc = jnp.sqrt(c)
            pn = _norm(p)
            return artanh(sc * pn) * p / (sc * pn)

        def mobius_add(x, y, c):
            x2 = jnp.sum(x * x, -1, keepdims=True)
            y2 = jnp.sum(y * y, -1, keepdims=True)
            xy = jnp.sum(x * y, -1, keepdims=True)
            num = (1 + 2 * c * xy + c * y2) * x + (1 - c * x2) * y
            denom = 1 + 2 * c * xy + c * c * x2 * y2
            return num / jnp.clip(denom, MIN_NORM, None)

        def mobius_matvec(m, x, c):
            sc = jnp.sqrt(c)
            xn = _norm(x)
            mx = x @ m.T
            mxn = _norm(mx)
            res = jnp.tanh(mxn / xn * artanh(sc * xn)) * mx / (mxn * sc)
            zero_rows = jnp.all(mx == 0, axis=-1, keepdims=True)
            return jnp.where(zero_rows, jnp.zeros_like(res), res)
        key = jax.random.key(seed)
        k1, k2, k3, k4 = jax.random.split(key, 4)
        N, din, dout = (8192, 128, 128)
        x = jax.random.normal(k1, (N, din), dtype=jnp.float32) * 0.01
        adj = jax.random.uniform(k2, (N, N), dtype=jnp.float32)
        adj = adj / jnp.sum(adj, axis=-1, keepdims=True)
        bound = math_bound = float(np.sqrt(2.0) * np.sqrt(6.0 / (din + dout)))
        weight = jax.random.uniform(k3, (dout, din), dtype=jnp.float32, minval=-bound, maxval=bound)
        bias = jax.random.normal(k4, (dout,), dtype=jnp.float32) * 0.01
        return {'x': x, 'adj': adj, 'weight': weight, 'bias': bias}
    _L0_gnn_all = _L0_gnn_setup()
    _L0_gnn_in = {k: v for k, v in _L0_gnn_all.items() if k in ('weight', 'bias')}
    del _L0_gnn_all

    def _L1_gnn_setup():
        import jax, jax.numpy as jnp
        import numpy as np
        N = 8192
        IN_F = 128
        OUT_F = 128
        TOP_K = 32
        key = jax.random.key(seed)
        kx, ka, kw, kb = jax.random.split(key, 4)
        x = jax.random.normal(kx, (N, IN_F), dtype=jnp.float32)
        adj = jax.random.uniform(ka, (N, N), dtype=jnp.float32)
        W = jax.random.normal(kw, (OUT_F, IN_F), dtype=jnp.float32) * (1.0 / np.sqrt(IN_F))
        b = jax.random.normal(kb, (OUT_F,), dtype=jnp.float32) * 0.01
        return {'x': x, 'adj': adj, 'W': W, 'b': b, 'top_k': TOP_K}
    _L1_gnn_all = _L1_gnn_setup()
    _L1_gnn_in = {k: v for k, v in _L1_gnn_all.items() if k in ('W', 'b')}
    del _L1_gnn_all

    def _L2_gnn_setup():
        import jax, jax.numpy as jnp
        import numpy as np
        N = 8192
        U = 128
        AVG_DEGREE = 32
        key = jax.random.key(seed)
        kx, ka, kw = jax.random.split(key, 3)
        x = jax.random.normal(kx, (N, U), dtype=jnp.float32)
        adj = (jax.random.uniform(ka, (N, N)) < AVG_DEGREE / N).astype(jnp.float32)
        W = jax.random.normal(kw, (U, U), dtype=jnp.float32) * 0.05
        b = jnp.zeros((U,), dtype=jnp.float32)
        return {'x': x, 'adj': adj, 'W': W, 'b': b}
    _L2_gnn_all = _L2_gnn_setup()
    _L2_gnn_in = {k: v for k, v in _L2_gnn_all.items() if k in ('W', 'b')}
    del _L2_gnn_all

    def _L3_gnn_setup():
        import jax, jax.numpy as jnp
        import numpy as np
        N = 8192
        F_IN = 128
        F_OUT = 128
        key = jax.random.key(seed)
        k1, k2, k3, k4 = jax.random.split(key, 4)
        x = jax.random.normal(k1, (N, F_IN), dtype=jnp.float32)
        adj = jax.random.uniform(k2, (N, N), dtype=jnp.float32)
        bound = 1.0 / np.sqrt(2 * F_IN)
        W = jax.random.uniform(k3, (F_OUT, 2 * F_IN), minval=-bound, maxval=bound, dtype=jnp.float32)
        b = jax.random.uniform(k4, (F_OUT,), minval=-bound, maxval=bound, dtype=jnp.float32)
        return {'x': x, 'adj': adj, 'W': W, 'b': b}
    _L3_gnn_all = _L3_gnn_setup()
    _L3_gnn_in = {k: v for k, v in _L3_gnn_all.items() if k in ('W', 'b')}
    del _L3_gnn_all
    return {'x': x, 'adj': adj, 'L0_gnn_weight': _L0_gnn_in['weight'], 'L0_gnn_bias': _L0_gnn_in['bias'], 'L1_gnn_W': _L1_gnn_in['W'], 'L1_gnn_b': _L1_gnn_in['b'], 'L2_gnn_W': _L2_gnn_in['W'], 'L2_gnn_b': _L2_gnn_in['b'], 'L3_gnn_W': _L3_gnn_in['W'], 'L3_gnn_b': _L3_gnn_in['b']}

def reference(x, adj, L0_gnn_weight, L0_gnn_bias, L1_gnn_W, L1_gnn_b, L2_gnn_W, L2_gnn_b, L3_gnn_W, L3_gnn_b):
    import jax
    import jax.numpy as jnp

    def _L0_gnn_ref(x, adj, weight, bias):
        import jax, jax.numpy as jnp
        import numpy as np
        MIN_NORM = 1e-15
        BALL_EPS = 0.004
        C_IN = 1.0
        C_OUT = 1.0

        def _norm(x):
            return jnp.clip(jnp.linalg.norm(x, axis=-1, keepdims=True), MIN_NORM, None)

        def artanh(x):
            return jnp.arctanh(jnp.clip(x, -1.0 + 1e-07, 1.0 - 1e-07))

        def proj(x, c):
            norm = _norm(x)
            maxnorm = (1.0 - BALL_EPS) / jnp.sqrt(c)
            return jnp.where(norm > maxnorm, x / norm * maxnorm, x)

        def expmap0(u, c):
            sc = jnp.sqrt(c)
            un = _norm(u)
            return jnp.tanh(sc * un) * u / (sc * un)

        def logmap0(p, c):
            sc = jnp.sqrt(c)
            pn = _norm(p)
            return artanh(sc * pn) * p / (sc * pn)

        def mobius_add(x, y, c):
            x2 = jnp.sum(x * x, -1, keepdims=True)
            y2 = jnp.sum(y * y, -1, keepdims=True)
            xy = jnp.sum(x * y, -1, keepdims=True)
            num = (1 + 2 * c * xy + c * y2) * x + (1 - c * x2) * y
            denom = 1 + 2 * c * xy + c * c * x2 * y2
            return num / jnp.clip(denom, MIN_NORM, None)

        def mobius_matvec(m, x, c):
            sc = jnp.sqrt(c)
            xn = _norm(x)
            mx = x @ m.T
            mxn = _norm(mx)
            res = jnp.tanh(mxn / xn * artanh(sc * xn)) * mx / (mxn * sc)
            zero_rows = jnp.all(mx == 0, axis=-1, keepdims=True)
            return jnp.where(zero_rows, jnp.zeros_like(res), res)
        mv = mobius_matvec(weight, x, C_IN)
        res = proj(mv, C_IN)
        hyp_bias = proj(expmap0(bias[None, :], C_IN), C_IN)
        h = proj(mobius_add(res, hyp_bias, C_IN), C_IN)
        xt = logmap0(h, C_IN)
        support_t = adj @ xt
        h = proj(expmap0(support_t, C_IN), C_IN)
        xt = jax.nn.relu(logmap0(h, C_IN))
        h = proj(expmap0(xt, C_OUT), C_OUT)
        return h

    def _L1_gnn_ref(x, adj, W, b, top_k):
        import jax, jax.numpy as jnp
        import numpy as np
        N = 8192
        IN_F = 128
        OUT_F = 128
        TOP_K = 32
        h = jnp.einsum('ni,oi->no', x, W) + b
        _, topk_idx = jax.lax.top_k(adj, top_k)
        h_agg = jnp.max(h[topk_idx], axis=1)
        return h_agg

    def _L2_gnn_ref(x, adj, W, b):
        import jax, jax.numpy as jnp
        import numpy as np
        N = 8192
        U = 128
        AVG_DEGREE = 32
        adj = jax.lax.stop_gradient(adj)
        neigh1 = adj @ x
        x1 = jax.nn.swish(neigh1 @ W + b)
        neigh2 = adj @ x1
        x2 = jax.nn.swish(neigh2 @ W + b)
        return x2

    def _L3_gnn_ref(x, adj, W, b):
        import jax, jax.numpy as jnp
        import numpy as np
        N = 8192
        F_IN = 128
        F_OUT = 128
        neigh = adj @ x
        W_self = W[:, :F_IN]
        W_neigh = W[:, F_IN:]
        return x @ W_self.T + neigh @ W_neigh.T + b
    h = jnp.maximum(_layernorm(x, axis=-1), 0.0)
    x = x + _L0_gnn_ref(h, adj, L0_gnn_weight, L0_gnn_bias)
    h = jnp.maximum(_layernorm(x, axis=-1), 0.0)
    x = x + _L1_gnn_ref(h, adj, L1_gnn_W, L1_gnn_b, 32)
    h = jnp.maximum(_layernorm(x, axis=-1), 0.0)
    x = x + _L2_gnn_ref(h, adj, L2_gnn_W, L2_gnn_b)
    h = jnp.maximum(_layernorm(x, axis=-1), 0.0)
    x = x + _L3_gnn_ref(h, adj, L3_gnn_W, L3_gnn_b)
    return x

_drawn_inputs = setup_inputs


def setup_inputs(seed=0):
    import zlib

    import numpy as np

    out = dict(_drawn_inputs(seed))
    spreads = {'L2_gnn_b': (0.0, 0.1)}
    factors = {'L0_gnn_bias': 8.0, 'L1_gnn_b': 5.604}
    for name, (base, spread) in spreads.items():
        noise = np.random.default_rng([zlib.crc32(name.encode()), seed]).standard_normal(out[name].shape)
        drawn = base * np.exp(spread * noise) if base else spread * noise
        out[name] = jnp.asarray(drawn.astype(out[name].dtype))
    for name, factor in factors.items():
        out[name] = (out[name] * factor).astype(out[name].dtype)
    return out
```

```python
import concourse.bass as bass
from concourse import mybir
from contextlib import ExitStack
import math
import numpy as np

P = 128


class Chain:

    def __init__(self, engine, semaphore, per_round):
        self.engine, self.semaphore, self.per_round = engine, semaphore, per_round

    def start(self, n):
        self.base, self.k = n * self.per_round, 0

    def step(self, instruction, apart=None):
        self.k += 1
        instruction.then_inc(self.semaphore, 1)
        self.engine.wait_ge(self.semaphore, self.base + self.k)
        if apart is not None:
            apart()

    def end(self):
        assert self.k == self.per_round, (self.k, self.per_round)


def gnn_program(nc, x, adj, adjT, weights, bias_rows, bias0_col, h1_rows, out):
    f32, u32 = mybir.dt.float32, mybir.dt.uint32
    ALU, ACT, AX = mybir.AluOpType, mybir.ActivationFunctionType, mybir.AxisListType

    N, D = x.shape
    NT = N // P
    W = 512
    T = W // P
    NB = N // W
    NSLOT = 4
    KPS = NT // NSLOT
    TOPK = 32
    LN_EPS = 1e-5
    MAXNORM = float(np.float32(1.0 - 0.004))
    ART_MAX = math.atanh(MAXNORM)
    ART_CLIP = float(np.float32(1.0 - 1e-7))
    TINY = 1e-15
    TINY2 = TINY * TINY
    SERIES_BELOW = 0.1
    LOWEST = -3.4028234663852886e38

    x_v = x.rearrange("(t p) c -> p t c", p=P)
    adjT_slot = adjT.rearrange("(s k p) i -> s p k i", s=NSLOT, p=P)
    h1_v = h1_rows.rearrange("(t p) c -> p t c", p=P)
    out_v = out.rearrange("(t p) c -> p t c", p=P)

    with ExitStack() as ctx:
        def sb(name, shape, dt=f32):
            return ctx.enter_context(nc.sbuf_tensor(name, shape, dt))

        def sem(name):
            return ctx.enter_context(nc.semaphore(name))

        ring = sb("ring", [P, NSLOT, KPS, W])
        resid = sb("resid", [P, NT, D])
        xa = sb("xa", [P, NT, D])
        xb = sb("xb", [P, NT, D])
        nat = sb("nat", [P, 2, N])
        gath = sb("gath", [P, 2, TOPK * D])
        topv = sb("topv", [P, TOPK])
        topi = sb("topi", [P, 2, TOPK], u32)
        hk = sb("hk", [P, 2, D])
        wt = sb("wt", [P, 6, D])
        bc = sb("bc", [P, 4, D])
        b0c = sb("b0c", [P, 1])
        ident = sb("ident", [P, P])
        hb = sb("hb", [P, D])
        hbc = sb("hbc", [P, 1])
        vcol = sb("vcol", [P, 1])
        bsc = sb("bsc", [P, 8])
        uT = sb("uT", [P, 2, W])
        hblk = sb("hblk", [P, T, D])
        hT = sb("hT", [P, W])
        rblk = sb("rblk", [P, T, D])
        yblk = sb("yblk", [P, T, D])
        sq_act = sb("sq_act", [P, T, D])
        sq_dve = sb("sq_dve", [P, T, D])
        stats = sb("stats", [P, T, 6])
        mv = sb("mv", [P, T, 2])
        lnv = sb("lnv", [P, 4, T])
        pn = sb("pn", [P, 3, NT])
        pv = sb("pv", [P, 24, NT])
        nb2 = sb("nb2", [P, 2, T])
        bv = sb("bv", [P, 10, T])
        gmax = sb("gmax", [P, D])
        ps = [ctx.enter_context(nc.psum_tensor(f"ps{b}", [P, W], f32)) for b in range(8)]
        BACK, HTP, WOUT, DOT = ps[2], ps[3], ps[4], ps[5]

        spare_dve, spare_pool = sem("spare_dve"), sem("spare_pool")
        x_in, consts, id_zero, id_ready = sem("x_in"), sem("consts"), sem("id_zero"), sem("id_ready")
        slot_full = [sem(f"slot_full{s}") for s in range(NSLOT)]
        slot_free = [sem(f"slot_free{s}") for s in range(NSLOT)]
        chain, bias_norm, bias_std, bias_tanh = sem("chain"), sem("bias_norm"), sem("bias_std"), sem("bias_tanh")
        hbc_ready, vcol_psum, vcol_ready = sem("hbc_ready"), sem("vcol_psum"), sem("vcol_ready")
        LN_KEYS = ("chain", "var", "std", "scale", "applied")
        ln = {k: sem(f"ln_{k}") for k in LN_KEYS}
        ln2 = {k: sem(f"ln2_{k}") for k in LN_KEYS}
        hTp_ready, hT_copied = sem("hTp_ready"), sem("hT_copied")
        wout_ready, wout_taken = sem("wout_ready"), sem("wout_taken")
        hnorm_done, mx_copied, mxnorm_done = sem("hnorm_done"), sem("mx_copied"), sem("mxnorm_done")
        mob = {k: (sem(f"mob_{k}_in"), sem(f"mob_{k}_out")) for k in ("norms", "ln_x", "tanh", "hn", "ln_h")}
        xa_scaled, xa_ready = sem("xa_scaled"), sem("xa_ready")
        acc_taken, back_ready, back_taken = sem("acc_taken"), sem("back_ready"), sem("back_taken")
        relu_ready = sem("relu_ready")
        p1_chain = sem("p1_chain")
        u_norms, u_std, vn_ready, vn_tanh = sem("u_norms"), sem("u_std"), sem("vn_ready"), sem("vn_tanh")
        x1_ready, hl_copied, hl_stored = sem("x1_ready"), sem("hl_copied"), sem("hl_stored")
        nat_in = [sem(f"nat_in{i}") for i in range(2)]
        top_chain, idx_ready = sem("top_chain"), sem("idx_ready")
        gathered = [sem(f"gathered{i}") for i in range(2)]
        gmax_ready, x2_ready = sem("gmax_ready"), sem("x2_ready")
        acc2_copied, y1_psum, y1_ready, xb_ready = sem("acc2_copied"), sem("y1_psum"), sem("y1_ready"), sem("xb_ready")
        silu_ready, x3_ready = sem("silu_ready"), sem("x3_ready")
        self_psum, self_ready, self_added = sem("self_psum"), sem("self_ready"), sem("self_added")
        h3_copied, out_ready, out_stored = sem("h3_copied"), sem("out_ready"), sem("out_stored")

        credited = [*slot_free, hT_copied, mx_copied, acc_taken, back_taken, wout_taken, self_ready, hTp_ready,
                    hnorm_done, mxnorm_done, back_ready, x1_ready, h3_copied, ln["applied"], ln2["applied"],
                    hl_copied, x2_ready, self_added, idx_ready, xa_ready, xb_ready]

        block = ctx.enter_context(nc.Block())

        def flat(ap):
            return ap.rearrange("p t c -> p (t c)")

        def blk(buf, b):
            return buf[:, b * T:(b + 1) * T, :] if isinstance(b, int) else buf[:, bass.ds(b * T, T), :]

        def tile(buf, t):
            return buf[:, t, :]

        def spread(row, count):
            return row.rearrange("p (o c) -> p o c", o=1).broadcast_to([P, count, D])

        def block_done(eng, product, b):
            eng.wait_ge(slot_free[NSLOT - 1], 1 + NB * product + b + 1)

        @block.sync
        def _(sp):
            sp.dma_start(resid[:, :, :], x_v).then_inc(x_in, 16)
            sp.dma_start(wt[:, :, :], weights.rearrange("w k c -> k w c")).then_inc(consts, 16)
            sp.dma_start(flat(bc[:, :, :]), bias_rows.partition_broadcast(P)).then_inc(consts, 16)
            sp.dma_start(b0c[:, :], bias0_col).then_inc(consts, 16)

            def load_blocks(product):
                with sp.Fori(0, NB) as b:
                    for s in range(NSLOT):
                        sp.wait_ge(slot_free[s], 1 + NB * product + b)
                        sp.dma_start(ring[:, s, :, :], adjT_slot[s][:, :, bass.ds(b * W, W)])\
                          .then_inc(slot_full[s], 16)

            load_blocks(0)
            with sp.Fori(0, NB) as r:
                for s in range(NSLOT):
                    sp.wait_ge(slot_free[s], 1 + NB + r)
                    sp.dma_start(ring[:, s, :, :].rearrange("p k i -> p (k i)"),
                                 adjT[bass.ds((r * NSLOT + s) * P, P), :]).then_inc(slot_full[s], 16)
            load_blocks(2)
            load_blocks(3)

        @block.tensor
        def _(pe):
            pe.wait_ge(id_ready, 1)
            pe.wait_ge(consts, 48)
            pe.wait_ge(hbc_ready, 1)
            nc.tensor.matmul(DOT[:, 8:9], wt[:, 1, :], hbc[:, :], start=True, stop=True).then_inc(vcol_psum, 1)
            pe.wait_ge(vcol_ready, 1)

            def transposes(dst, src, ready):
                for j in range(T):
                    last = nc.tensor.transpose(dst[:, j * P:(j + 1) * P], src(j), ident[:, :])
                last.then_inc(ready, 1)

            def weigh(dst, srcT, w, ready):
                for j in range(T):
                    last = nc.tensor.matmul(dst[:, j * P:(j + 1) * P], srcT[:, j * P:(j + 1) * P], wt[:, w, :],
                                            start=True, stop=True)
                if ready is not None:
                    last.then_inc(ready, 1)

            def h_transposed(n):
                pe.wait_ge(ln["applied"], 1 + n + 1)
                pe.wait_ge(hT_copied, 1 + n)
                transposes(HTP, lambda j: hblk[:, j, :], hTp_ready)

            with pe.Fori(0, NB) as g:
                h_transposed(g)
                pe.wait_ge(hT_copied, 1 + g + 1)
                pe.wait_ge(mx_copied, 1 + g)
                weigh(WOUT, hT, 0, None)
                for j in range(T):
                    last = nc.tensor.matmul(DOT[:, j:j + 1], hT[:, j * P:(j + 1) * P], vcol[:, :],
                                            start=True, stop=True)
                last.then_inc(wout_ready, 1)

            def product_block(b, bank, operand, product, operand_ready, steps, bank_waits):
                for s, v in bank_waits:
                    pe.wait_ge(s, v)
                for k in range(NT):
                    if k % KPS == 0:
                        pe.wait_ge(slot_full[k // KPS], 16 * (NB * product + b + 1))
                    if k % T == 0 and operand_ready is not None:
                        pe.wait_ge(operand_ready, 1 + k // T + 1)
                    last = nc.tensor.matmul(ps[bank][:, :], operand[:, k, :], ring[:, k // KPS, k % KPS, :],
                                            start=(k == 0), stop=(k == NT - 1))
                    if k % KPS == KPS - 1:
                        last.then_inc(slot_free[k // KPS], 1)
                    if k in steps:
                        steps[k]()

            def product_blocks(n0, product, operand, operand_ready, steps, bank_waits):
                product_block(0, 0, operand, product, operand_ready, {}, bank_waits)
                with pe.Fori(0, NB // 2 - 1) as i:
                    for d in (1, 2):
                        b = 2 * i + d
                        product_block(b, d % 2, operand, product, None, steps(b - 1), [(acc_taken, b + n0)])
                product_block(NB - 1, 1, operand, product, None, steps(NB - 2), [(acc_taken, n0 + NB - 1)])
                for step in steps(NB - 1).values():
                    step()

            def u_back(b):
                pe.wait_ge(acc_taken, 1 + b + 1)
                pe.wait_ge(back_taken, 1 + b)
                transposes(BACK, lambda j: uT[:, 0, j * P:(j + 1) * P], back_ready)

            def h1_product(b):
                pe.wait_ge(hT_copied, 1 + NB + b + 1)
                pe.wait_ge(wout_taken, 1 + b)
                weigh(WOUT, hT, 2, wout_ready)

            def steps1(b):
                return {6: lambda: u_back(b), 20: lambda: h_transposed(b + NB), 26: lambda: h1_product(b)}

            pe.wait_ge(mx_copied, 1 + NB)
            product_blocks(0, 0, xa, xa_ready, steps1, [])

            pe.wait_ge(back_taken, 1 + NB)
            pe.wait_ge(hT_copied, 1 + 2 * NB)
            pe.wait_ge(wout_taken, 1 + NB)

            def product2(r, first, final):
                for s in range(NSLOT):
                    pe.wait_ge(ln2["applied"], 1 + r * NSLOT + s + 1)
                    pe.wait_ge(slot_full[s], 16 * (NB + r + 1))
                    for b in range(NB):
                        last = nc.tensor.matmul(ps[b][:, :], hk[:, s % 2, :], ring[:, s, b, :],
                                                start=(first and s == 0), stop=(final and s == NSLOT - 1))
                    last.then_inc(slot_free[s], 1)
            product2(0, True, False)
            with pe.Fori(1, NB - 1) as r:
                product2(r, False, False)
            product2(NB - 1, False, True)

            for b in range(NB):
                pe.wait_ge(acc2_copied, b + 1)
                weigh(ps[b], uT[:, b % 2, :], 3, y1_psum)

            def weigh_neighbours(n, w):
                pe.wait_ge(acc_taken, 1 + n + NB + 1)
                pe.wait_ge(wout_taken, 1 + n + NB)
                weigh(WOUT, uT[:, 0, :], w, wout_ready)

            def self_product(b):
                pe.wait_ge(hT_copied, 1 + 2 * NB + b + 1)
                pe.wait_ge(self_ready, 1 + b)
                weigh(BACK, hT, 4, self_psum)

            def steps3(b):
                return {6: lambda: weigh_neighbours(b, 3), 20: lambda: h_transposed(b + 2 * NB),
                        26: lambda: self_product(b)}
            product_blocks(NB, 2, xb, xb_ready, steps3, [(y1_ready, NB)])

            product_blocks(2 * NB, 3, xa, h3_copied, lambda b: {6: lambda: weigh_neighbours(b + NB, 5)},
                           [(acc_taken, 2 * NB)])

        @block.scalar
        def _(act):
            act.wait_ge(bias_norm, 1)
            nc.scalar.activation(bsc[:, 2:3], bsc[:, 1:2], ACT.Sqrt).then_inc(bias_std, 1)
            act.wait_ge(bias_std, 2)
            nc.scalar.activation(bsc[:, 4:5], bsc[:, 3:4], ACT.Tanh).then_inc(bias_tanh, 1)

            def ln_std(n, s, width):
                act.wait_ge(s["var"], n + 1)
                nc.scalar.activation(lnv[:, 1, 0:width], lnv[:, 0, 0:width], ACT.Sqrt).then_inc(s["std"], 1)
                act.wait_ge(s["scale"], n + 1)

            def h_block(n, b):
                ln_std(n, ln, T)
                act.wait_ge(hTp_ready, 1 + n)
                for j in range(T):
                    last = nc.scalar.activation(hblk[:, j, :], tile(resid, b * T + j), ACT.Relu,
                                                bias=lnv[:, 3, j:j + 1], scale=lnv[:, 2, j:j + 1])
                last.then_inc(ln["applied"], 1)

            def hT_copy(n):
                act.wait_ge(hTp_ready, 1 + n + 1)
                nc.scalar.activation(hT[:, :], HTP[:, :], ACT.Copy).then_inc(hT_copied, 1)

            with act.Fori(0, NB) as g:
                act.wait_ge(hnorm_done, 1 + g)
                h_block(g, g)
                hT_copy(g)
                act.wait_ge(wout_ready, g + 1)
                nc.scalar.activation(flat(blk(xb, g)), WOUT[:, :], ACT.Copy)
                nc.scalar.activation(pn[:, 2, bass.ds(g * T, T)], DOT[:, 0:T], ACT.Copy).then_inc(mx_copied, 1)

            def function(key, dst, src, func):
                act.wait_ge(mob[key][0], 1)
                nc.scalar.activation(dst, src, func).then_inc(mob[key][1], 1)
            function("norms", pv[:, 2:4, :], pv[:, 0:2, :], ACT.Sqrt)
            function("ln_x", pv[:, 6:8, :], pv[:, 4:6, :], ACT.Ln)
            function("tanh", pv[:, 13, :], pv[:, 12, :], ACT.Tanh)
            function("hn", pv[:, 1, :], pv[:, 0, :], ACT.Sqrt)
            function("ln_h", pv[:, 6:8, :], pv[:, 4:6, :], ACT.Ln)

            def acc_copy(product, b, bank):
                block_done(act, product, b)
                nc.scalar.activation(uT[:, 0, :], ps[bank][:, :], ACT.Copy).then_inc(acc_taken, 1)

            def after1(b, bank):
                act.wait_ge(back_ready, 1 + b)
                acc_copy(0, b, bank)
                act.wait_ge(back_ready, 1 + b + 1)
                act.wait_ge(x1_ready, 1 + b)
                nc.scalar.activation(flat(rblk[:, :, :]), BACK[:, :], ACT.Relu).then_inc(relu_ready, 1)
                for j in range(T):
                    last = nc.scalar.activation(sq_act[:, j, :], BACK[:, j * P:(j + 1) * P], ACT.Square,
                                                accum_out=nb2[:, 0, j:j + 1])
                last.then_inc(back_taken, 1)
                act.wait_ge(u_norms, b + 1)
                nc.scalar.activation(bv[:, 2:4, :], bv[:, 0:2, :], ACT.Sqrt).then_inc(u_std, 1)
                act.wait_ge(vn_ready, b + 1)
                nc.scalar.activation(bv[:, 7, :], bv[:, 6, :], ACT.Tanh).then_inc(vn_tanh, 1)
                h_block(b + NB, b)
                hT_copy(b + NB)
            with act.Fori(0, NB // 2) as i:
                after1(2 * i, 0)
                after1(2 * i + 1, 1)

            def nat_load(t, half):
                act.dma_start(nat[:, half, :], adj[bass.ds(t * P, P), :]).then_inc(nat_in[half], 16)

            def h2_tile(r, s):
                t = r * NSLOT + s
                ln_std(t, ln2, 1)
                if s >= 2:
                    act.wait_ge(slot_free[s - 2], 1 + NB + r + 1)
                else:
                    act.wait_ge(slot_free[s + 2], 1 + NB + r)
                nc.scalar.activation(hk[:, s % 2, :], tile(resid, t), ACT.Relu, bias=lnv[:, 3, 0:1],
                                     scale=lnv[:, 2, 0:1]).then_inc(ln2["applied"], 1)
            act.dma_start(nat[:, 0, :], adj[0:P, :]).then_inc(nat_in[0], 16)
            act.dma_start(nat[:, 1, :], adj[P:2 * P, :]).then_inc(nat_in[1], 16)
            with act.Fori(0, NB - 1) as r:
                for s in range(NSLOT):
                    act.wait_ge(idx_ready, 1 + r * NSLOT + s + 1)
                    nat_load(r * NSLOT + s + 2, s % 2)
                    h2_tile(r, s)
            for s in range(NSLOT):
                if s < 2:
                    act.wait_ge(idx_ready, 1 + NT - NSLOT + s + 1)
                    act.dma_start(nat[:, s, :], adj[(NT - 2 + s) * P:(NT - 1 + s) * P, :]).then_inc(nat_in[s], 16)
                h2_tile(NB - 1, s)

            def silu1(b):
                act.wait_ge(y1_ready, b + 1)
                nc.scalar.activation(blk(xb, b), (yblk, rblk)[b % 2][:, :, :], ACT.Silu).then_inc(xb_ready, 1)
            block_done(act, 1, NB - 1)
            for b in range(NB):
                if b >= 2:
                    act.wait_ge(y1_psum, b - 1)
                nc.scalar.activation(uT[:, b % 2, :], ps[b][:, :], ACT.Copy).then_inc(acc2_copied, 1)
                if b:
                    silu1(b - 1)
            silu1(NB - 1)

            def after3(b, bank):
                act.wait_ge(wout_ready, 2 * NB + b)
                acc_copy(2, b, bank)
                act.wait_ge(wout_taken, 1 + b + NB + 1)
                nc.scalar.activation(rblk[:, :, :], yblk[:, :, :], ACT.Silu).then_inc(silu_ready, 1)
                act.wait_ge(h3_copied, 1 + b)
                h_block(b + 2 * NB, b)
                hT_copy(b + 2 * NB)
            act.wait_ge(y1_psum, NB)
            with act.Fori(0, NB // 2) as i:
                after3(2 * i, 0)
                after3(2 * i + 1, 1)

            with act.Fori(0, NB // 2) as i:
                for bank in range(2):
                    act.wait_ge(wout_ready, 2 * i + bank + 3 * NB)
                    acc_copy(3, 2 * i + bank, bank)

        @block.vector
        def _(dve):
            V = nc.vector
            line = Chain(dve, chain, 0)
            line.start(0)
            go = line.step

            def row_norm2(acc, a, j=0):
                return V.scalar_tensor_tensor(out=sq_dve[:, j, :], in0=a, scalar=1.0, in1=a,
                                              op0=ALU.mult, op1=ALU.mult, accum_out=acc)

            dve.wait_ge(consts, 48)
            go(row_norm2(bsc[:, 0:1], bc[:, 0, :]))
            V.tensor_scalar(bsc[:, 1:2], bsc[:, 0:1], TINY2, None, ALU.max).then_inc(bias_norm, 1)
            dve.wait_ge(bias_std, 1)
            V.tensor_scalar(bsc[:, 3:4], bsc[:, 2:3], TINY, None, ALU.max).then_inc(bias_std, 1)
            dve.wait_ge(bias_std, 2)
            go(V.reciprocal(bsc[:, 5:6], bsc[:, 3:4]))
            dve.wait_ge(bias_tanh, 1)
            go(V.scalar_tensor_tensor(out=bsc[:, 6:7], in0=bsc[:, 4:5], scalar=MAXNORM, in1=bsc[:, 5:6],
                                      op0=ALU.min, op1=ALU.mult))
            V.tensor_scalar(hbc[:, :], b0c[:, :], bsc[:, 6:7], None, ALU.mult).then_inc(hbc_ready, 1)
            go(V.tensor_scalar(hb[:, :], bc[:, 0, :], bsc[:, 6:7], None, ALU.mult))
            go(row_norm2(bsc[:, 7:8], hb[:, :]))
            dve.wait_ge(vcol_psum, 1)
            V.tensor_copy(vcol[:, :], DOT[:, 8:9]).then_inc(vcol_ready, 1)

            def apart():
                dve.sem_inc(spare_dve, 1)

            ln_chain = {id(s): Chain(dve, s["chain"], 3) for s in (ln, ln2)}

            def ln_stats(n, s, src):
                c, width = ln_chain[id(s)], len(src)
                c.start(n)
                apart()
                for j, a in enumerate(src):
                    last = V.bn_stats(stats[:, j, :], a)
                c.step(last, apart)
                for j in range(width):
                    last = V.bn_aggr(mv[:, j, :], stats[:, j, :])
                c.step(last)
                dve.wait_ge(s["applied"], 1 + n)
                V.tensor_scalar(lnv[:, 0, 0:width], mv[:, 0:width, 1], LN_EPS, None, ALU.add).then_inc(s["var"], 1)
                dve.wait_ge(s["std"], n + 1)
                c.step(V.reciprocal(lnv[:, 2, 0:width], lnv[:, 1, 0:width]))
                V.scalar_tensor_tensor(out=lnv[:, 3, 0:width], in0=mv[:, 0:width, 0], scalar=-1.0,
                                       in1=lnv[:, 2, 0:width], op0=ALU.mult, op1=ALU.mult).then_inc(s["scale"], 1)
                c.end()

            def resid_tiles(b):
                return [tile(resid, b * T + j) for j in range(T)]

            def h0_norms(g, before):
                dve.wait_ge(ln["applied"], 1 + g + 1)
                dve.wait_ge(mxnorm_done, 1 + before)
                for j in range(T):
                    last = row_norm2(pn[:, 0, bass.ds(g * T + j, 1)], hblk[:, j, :], j)
                last.then_inc(hnorm_done, 1)

            def mx_norms(g, before):
                dve.wait_ge(mx_copied, 1 + g + 1)
                dve.wait_ge(hnorm_done, 1 + before)
                dve.wait_ge(mxnorm_done, 1 + g)
                for j in range(T):
                    last = row_norm2(pn[:, 1, bass.ds(g * T + j, 1)], tile(xb, g * T + j), j)
                last.then_inc(mxnorm_done, 1)

            dve.wait_ge(x_in, 16)
            ln_stats(0, ln, resid_tiles(0))
            h0_norms(0, 0)
            with dve.Fori(1, NB) as g:
                ln_stats(g, ln, resid_tiles(g))
                h0_norms(g, g - 1)
                mx_norms(g - 1, g + 1)
            mx_norms(NB - 1, NB)
            dve.wait_ge(hnorm_done, 1 + NB)
            dve.wait_ge(mxnorm_done, 1 + NB)

            def col(i):
                return pv[:, i, :]

            def ts(dst, a, s1, op1, s2=None, op2=None):
                go(V.tensor_scalar(dst, a, s1, s2, op1, op2) if op2 is not None else
                   V.tensor_scalar(dst, a, s1, None, op1))

            def stt(dst, a, s, b, op1, op2):
                go(V.scalar_tensor_tensor(out=dst, in0=a, scalar=s, in1=b, op0=op1, op1=op2))

            def tt(dst, a, b, op):
                go(V.tensor_tensor(dst, a, b, op))

            def artanh_ratio(dst, n, clip, key):
                c, c2, series, inv, logs, small = col(18), col(19), col(20), col(21), col(22), col(23)
                ts(c, n, clip, ALU.min)
                ts(col(4), c, 1.0, ALU.add)
                V.tensor_scalar(col(5), c, -1.0, 1.0, ALU.mult, ALU.add).then_inc(mob[key][0], 1)
                tt(c2, c, c, ALU.mult)
                ts(series, c2, 1.0 / 9, ALU.mult)
                stt(series, series, 1.0 / 7, c2, ALU.add, ALU.mult)
                stt(series, series, 1.0 / 5, c2, ALU.add, ALU.mult)
                stt(series, series, 1.0 / 3, c2, ALU.add, ALU.mult)
                go(V.reciprocal(inv, n))
                ts(small, c, SERIES_BELOW, ALU.is_lt)
                dve.wait_ge(mob[key][1], 1)
                tt(logs, col(6), col(7), ALU.subtract)
                stt(logs, logs, 0.5, inv, ALU.mult, ALU.mult)
                stt(series, series, 1.0, logs, ALU.add, ALU.subtract)
                tt(series, series, small, ALU.mult)
                tt(dst, logs, series, ALU.add)

            hb2 = bsc[:, 7:8]
            xn, mxn, ratio, s1, q, xy = col(8), col(9), col(10), col(11), pn[:, 1, :], col(14)
            V.tensor_scalar(pv[:, 0:2, :], pn[:, 0:2, :], TINY2, None, ALU.max).then_inc(mob["norms"][0], 1)
            dve.wait_ge(mob["norms"][1], 1)
            ts(pv[:, 8:10, :], pv[:, 2:4, :], TINY, ALU.max)
            artanh_ratio(ratio, xn, ART_CLIP, "ln_x")
            V.tensor_tensor(col(12), ratio, mxn, ALU.mult).then_inc(mob["tanh"][0], 1)
            go(V.reciprocal(col(15), mxn))
            dve.wait_ge(mob["tanh"][1], 1)
            stt(s1, col(13), MAXNORM, col(15), ALU.min, ALU.mult)
            tt(xy, s1, pn[:, 2, :], ALU.mult)
            tt(col(15), s1, s1, ALU.mult)
            tt(col(15), col(15), q, ALU.mult)
            ts(col(16), xy, 2.0, ALU.mult, 1.0, ALU.add)
            stt(col(17), col(15), hb2, col(16), ALU.mult, ALU.add)
            ts(col(17), col(17), TINY, ALU.max)
            go(V.reciprocal(col(17), col(17)))
            stt(col(16), col(16), hb2, col(17), ALU.add, ALU.mult)
            alpha, beta = col(12), col(13)
            tt(alpha, col(16), s1, ALU.mult)
            ts(col(15), col(15), -1.0, ALU.mult, 1.0, ALU.add)
            tt(beta, col(15), col(17), ALU.mult)
            tt(col(16), alpha, alpha, ALU.mult)
            tt(col(16), col(16), q, ALU.mult)
            tt(col(17), alpha, beta, ALU.mult)
            tt(col(17), col(17), pn[:, 2, :], ALU.mult)
            stt(col(16), col(17), 2.0, col(16), ALU.mult, ALU.add)
            tt(col(17), beta, beta, ALU.mult)
            stt(col(16), col(17), hb2, col(16), ALU.mult, ALU.add)
            V.tensor_scalar(col(0), col(16), TINY2, None, ALU.max).then_inc(mob["hn"][0], 1)
            dve.wait_ge(mob["hn"][1], 1)
            ts(xn, col(1), TINY, ALU.max)
            artanh_ratio(ratio, xn, MAXNORM, "ln_h")
            tt(alpha, alpha, ratio, ALU.mult)
            tt(beta, beta, ratio, ALU.mult)

            with dve.Fori(0, NB) as g:
                for j in range(T):
                    last = V.tensor_scalar(tile(xb, g * T + j), tile(xb, g * T + j), alpha[:, bass.ds(g * T + j, 1)],
                                           None, ALU.mult)
                last.then_inc(xa_scaled, 1)
                dve.wait_ge(xa_scaled, g + 1)
                for j in range(T):
                    last = V.scalar_tensor_tensor(out=tile(xa, g * T + j), in0=hb[:, :],
                                                  scalar=beta[:, bass.ds(g * T + j, 1)], in1=tile(xb, g * T + j),
                                                  op0=ALU.mult, op1=ALU.add)
                last.then_inc(xa_ready, 1)

            c1 = Chain(dve, p1_chain, 8)

            def after1(b):
                c1.start(b)
                un, rn, inv, delta, vn, th = (bv[:, i, :] for i in (2, 3, 4, 5, 6, 7))
                dve.wait_ge(relu_ready, b + 1)
                for j in range(T):
                    last = row_norm2(nb2[:, 1, j:j + 1], rblk[:, j, :], j)
                c1.step(last)
                dve.wait_ge(back_taken, 1 + b + 1)
                V.tensor_scalar(bv[:, 0:2, :], nb2[:, :, :], TINY2, None, ALU.max).then_inc(u_norms, 1)
                dve.wait_ge(u_std, b + 1)
                c1.step(V.tensor_scalar(un, un, TINY, None, ALU.max))
                c1.step(V.reciprocal(inv, un))
                c1.step(V.scalar_tensor_tensor(out=delta, in0=un, scalar=ART_MAX, in1=inv, op0=ALU.min, op1=ALU.mult))
                c1.step(V.tensor_tensor(vn, delta, rn, ALU.mult))
                V.tensor_scalar(vn, vn, TINY, None, ALU.max).then_inc(vn_ready, 1)
                dve.wait_ge(vn_ready, b + 1)
                c1.step(V.reciprocal(inv, vn))
                c1.step(V.tensor_tensor(inv, inv, delta, ALU.mult))
                dve.wait_ge(vn_tanh, b + 1)
                c1.step(V.scalar_tensor_tensor(out=inv, in0=th, scalar=MAXNORM, in1=inv, op0=ALU.min, op1=ALU.mult))
                for j in range(T):
                    last = V.scalar_tensor_tensor(out=tile(resid, b * T + j), in0=rblk[:, j, :], scalar=inv[:, j:j + 1],
                                                  in1=tile(resid, b * T + j), op0=ALU.mult, op1=ALU.add)
                last.then_inc(x1_ready, 1)
                dve.wait_ge(x1_ready, 1 + b + 1)
                ln_stats(b + NB, ln, resid_tiles(b))
                dve.wait_ge(wout_ready, b + NB + 1)
                dve.wait_ge(hl_copied, 1 + b)
                V.tensor_tensor(yblk[:, :, :], WOUT[:, :].rearrange("p (t c) -> p t c", c=D), spread(bc[:, 1, :], T),
                                ALU.add).then_inc(wout_taken, 1)
                c1.end()
            with dve.Fori(0, NB) as b:
                after1(b)

            ct = Chain(dve, top_chain, TOPK // 8 * 2 + (TOPK // 8 - 1))

            def search(i, half):
                t = 2 * i + half
                ct.start(t)
                dve.wait_ge(nat_in[half], 16 * (i + 1))
                row = nat[:, half, :]
                apart()
                for r in range(TOPK // 8):
                    eight = slice(8 * r, 8 * r + 8)
                    ct.step(V.max(topv[:, eight], row), apart)
                    ct.step(V.max_index(topi[:, half, eight], topv[:, eight], row), apart)
                    if r < TOPK // 8 - 1:
                        ct.step(V.match_replace(row, topv[:, eight], row, LOWEST), apart)
                dve.sem_inc(idx_ready, 1)
                ct.end()

            def use_gathered(i, half):
                t = 2 * i + half
                dve.wait_ge(gathered[half], 16 * TOPK * (i + 1))
                V.tensor_reduce(gmax[:, :], gath[:, half, :].rearrange("p (s c) -> p c s", c=D), axis=AX.X,
                                op=ALU.max).then_inc(gmax_ready, 1)
                dve.wait_ge(gmax_ready, t + 1)
                V.tensor_tensor(tile(resid, t), tile(resid, t), gmax[:, :], ALU.add).then_inc(x2_ready, 1)
                dve.wait_ge(x2_ready, 1 + t + 1)
                ln_stats(t, ln2, [tile(resid, t)])

            search(0, 0)
            with dve.Fori(0, NT // 2 - 1) as i:
                search(i, 1)
                use_gathered(i, 0)
                search(i + 1, 0)
                use_gathered(i, 1)
            search(NT // 2 - 1, 1)
            use_gathered(NT // 2 - 1, 0)
            use_gathered(NT // 2 - 1, 1)

            for b in range(NB):
                dve.wait_ge(y1_psum, b + 1)
                if b >= 2:
                    dve.wait_ge(xb_ready, 1 + b - 1)
                V.tensor_tensor((yblk, rblk)[b % 2][:, :, :], ps[b][:, :].rearrange("p (t c) -> p t c", c=D),
                                spread(bc[:, 2, :], T), ALU.add).then_inc(y1_ready, 1)

            def after3(b):
                dve.wait_ge(wout_ready, b + 2 * NB + 1)
                dve.wait_ge(self_added, 1 + b)
                V.tensor_tensor(yblk[:, :, :], WOUT[:, :].rearrange("p (t c) -> p t c", c=D), spread(bc[:, 2, :], T),
                                ALU.add).then_inc(wout_taken, 1)
                dve.wait_ge(silu_ready, b + 1)
                V.tensor_tensor(blk(resid, b), blk(resid, b), rblk[:, :, :], ALU.add).then_inc(x3_ready, 1)
                dve.wait_ge(x3_ready, b + 1)
                ln_stats(b + 2 * NB, ln, resid_tiles(b))
                dve.wait_ge(self_psum, b + 1)
                V.tensor_tensor(yblk[:, :, :], BACK[:, :].rearrange("p (t c) -> p t c", c=D), spread(bc[:, 3, :], T),
                                ALU.add).then_inc(self_ready, 1)
                dve.wait_ge(self_ready, 1 + b + 1)
                V.tensor_tensor(blk(resid, b), blk(resid, b), yblk[:, :, :], ALU.add).then_inc(self_added, 1)
            dve.wait_ge(xb_ready, 1 + NB)
            with dve.Fori(0, NB) as b:
                after3(b)
            dve.wait_ge(self_added, 1 + NB)

            with dve.Fori(0, NB) as b:
                dve.wait_ge(wout_ready, b + 3 * NB + 1)
                V.tensor_tensor(blk(xb, b), WOUT[:, :].rearrange("p (t c) -> p t c", c=D), blk(resid, b),
                                ALU.add).then_inc(wout_taken, 1)

        @block.gpsimd
        def _(pool):
            for s in credited:
                pool.sem_inc(s, 1)
            nc.gpsimd.memset(ident[:, :], 0.0).then_inc(id_zero, 1)
            pool.wait_ge(id_zero, 1)
            nc.gpsimd.affine_select(out=ident[:, :], in_=ident[:, :], compare_op=ALU.not_equal, fill=1.0, base=0,
                                    pattern=[[-1, P]], channel_multiplier=1).then_inc(id_ready, 1)
            with pool.Fori(0, NB) as b:
                pool.wait_ge(wout_taken, 1 + b + 1)
                pool.dma_start(h1_v[:, bass.ds(b * T, T), :], yblk[:, :, :]).then_inc(hl_stored, 16)
                pool.wait_ge(hl_stored, 16 * (b + 1))
                pool.sem_inc(hl_copied, 1)
            pool.wait_ge(hl_stored, 16 * NB)

            with pool.Fori(0, NT // 2) as i:
                for half in range(2):
                    pool.wait_ge(idx_ready, 1 + 2 * i + half + 1)
                    pool.wait_ge(x2_ready, 1 + 2 * i)
                    pool.sem_inc(spare_pool, 1)
                    for k in range(TOPK):
                        pool.indirect_dma_start(gath[:, half, k * D:(k + 1) * D], None, h1_rows,
                                                bass.IndirectOffsetOnAxis(ap=topi[:, half, k:k + 1], axis=0))\
                            .then_inc(gathered[half], 16)

            with pool.Fori(0, NB) as b:
                pool.wait_ge(ln["applied"], 1 + b + 2 * NB + 1)
                nc.gpsimd.tensor_copy(blk(xa, b), hblk[:, :, :]).then_inc(h3_copied, 1)
            with pool.Fori(0, NB) as b:
                pool.wait_ge(wout_taken, 1 + b + 2 * NB + 1)
                pool.dma_start(out_v[:, bass.ds(b * T, T), :], blk(xb, b)).then_inc(out_stored, 16)
            pool.wait_ge(out_stored, 16 * NB)


def kernel(x, adj, L0_gnn_weight, L0_gnn_bias, L1_gnn_W, L1_gnn_b, L2_gnn_W, L2_gnn_b, L3_gnn_W, L3_gnn_b):
    import concourse.bacc as _bacc
    from concourse.bass_utils import run_bass_kernel_spmd as _run

    x, adj, w0, w1, w2, w3 = (np.asarray(a) for a in (x, adj, L0_gnn_weight, L1_gnn_W, L2_gnn_W, L3_gnn_W))
    D = x.shape[1]
    arrays = {
        "x": np.ascontiguousarray(x),
        "adj": np.ascontiguousarray(adj),
        "adjT": np.ascontiguousarray(adj.T),
        "weights": np.stack([w0.T, w0, w1.T, w2, w3[:, :D].T, w3[:, D:].T]),
        "bias_rows": np.concatenate([np.asarray(b) for b in (L0_gnn_bias, L1_gnn_b, L2_gnn_b, L3_gnn_b)]),
        "bias0_col": np.ascontiguousarray(np.asarray(L0_gnn_bias).reshape(D, 1)),
    }
    nc = _bacc.Bacc("TRN2", target_bir_lowering=False, num_devices=1)
    args = [nc.dram_tensor(n, a.shape, mybir.dt.from_np(a.dtype), kind="ExternalInput").ap() for n, a in arrays.items()]
    h1_rows = nc.dram_tensor("h1_rows", x.shape, mybir.dt.float32, kind="Internal").ap()
    out = nc.dram_tensor("out", x.shape, mybir.dt.float32, kind="ExternalOutput").ap()
    gnn_program(nc, *args, h1_rows, out)
    return _run(nc, [arrays], core_ids=[0]).results[0]["out"]
```
